# Optimizing a Trainium2 kernel written in Bass

```python
import numpy as np
import jax
import jax.numpy as jnp

def _softmax(x, axis=-1):
    return jax.nn.softmax(x, axis=axis)

def _gelu(x):
    return jax.nn.gelu(x, approximate=True)

def _silu(x):
    return jax.nn.silu(x)

def _sigmoid(x):
    return jax.nn.sigmoid(x)

def _layernorm(x, axis=-1, eps=1e-05):
    m = jnp.mean(x, axis=axis, keepdims=True)
    v = jnp.var(x, axis=axis, keepdims=True)
    return (x - m) / jnp.sqrt(v + eps)

def _scatter_add(tgt, idx, src, axis=0):
    return tgt.at[idx].add(src)

def _segment_sum(src, seg, n):
    return jax.ops.segment_sum(src, seg, n)
kernel_name = 'mk_adaln_d1_jaxref_r8_cbb38b'

def setup_inputs(seed: int=0):
    np.random.seed(seed)
    _w = jnp.asarray

    def _L0_attn_setup():
        import jax, jax.numpy as jnp
        import numpy as np
        import math
        D = 128
        H = 16
        HEAD_D = D // H
        T = 256
        B = 4
        key = jax.random.key(seed)
        k1, k2, k3 = jax.random.split(key, 3)
        x = jax.random.normal(k1, (B, T, D), dtype=jnp.float32)
        w_attn = jax.random.normal(k2, (D, D + 2 * HEAD_D), dtype=jnp.float32) * (1.0 / math.sqrt(D))
        w_proj = jax.random.normal(k3, (D, D), dtype=jnp.float32) * (1.0 / math.sqrt(D))
        return {'x': x, 'w_attn': w_attn, 'w_proj': w_proj}
    _L0_attn_in = _L0_attn_setup()

    def _L0_ffn_setup():
        import jax, jax.numpy as jnp
        import numpy as np
        B, S, D, H, E, K = (2, 128, 128, 64, 16, 4)
        HS = 2 * H

        def silu(z):
            return z * jax.nn.sigmoid(z)
        key = jax.random.key(seed)
        ks = jax.random.split(key, 8)
        sc = lambda fan_in: 1.0 / np.sqrt(fan_in)
        x = jax.random.normal(ks[0], (B, S, D), jnp.float32)
        gate_w = jax.random.normal(ks[1], (E, D), jnp.float32) * sc(D)
        ws_in = jax.random.normal(ks[2], (D, HS), jnp.float32) * sc(D)
        vs_in = jax.random.normal(ks[3], (D, HS), jnp.float32) * sc(D)
        ws_out = jax.random.normal(ks[4], (HS, D), jnp.float32) * sc(HS)
        e_win = jax.random.normal(ks[5], (E, D, H), jnp.float32) * sc(D)
        e_vin = jax.random.normal(ks[6], (E, D, H), jnp.float32) * sc(D)
        e_wout = jax.random.normal(ks[7], (E, H, D), jnp.float32) * sc(H)
        return {'x': x, 'gate_w': gate_w, 'ws_in': ws_in, 'vs_in': vs_in, 'ws_out': ws_out, 'e_win': e_win, 'e_vin': e_vin, 'e_wout': e_wout}
    _L0_ffn_in = _L0_ffn_setup()
    _L0_c = _w((lambda *s: np.random.randn(*s).astype(np.float32) * 0.05)(2, 128))
    _L0_wmod = _w((lambda *s: np.random.randn(*s).astype(np.float32) * 0.05)(128, 6 * 128) * 128 ** (-0.5))
    _d = {'L0_attn_x': _L0_attn_in['x'], 'L0_attn_w_attn': _L0_attn_in['w_attn'], 'L0_attn_w_proj': _L0_attn_in['w_proj'], 'L0_ffn_gate_w': _L0_ffn_in['gate_w'], 'L0_ffn_ws_in': _L0_ffn_in['ws_in'], 'L0_ffn_vs_in': _L0_ffn_in['vs_in'], 'L0_ffn_ws_out': _L0_ffn_in['ws_out'], 'L0_ffn_e_win': _L0_ffn_in['e_win'], 'L0_ffn_e_vin': _L0_ffn_in['e_vin'], 'L0_ffn_e_wout': _L0_ffn_in['e_wout'], 'L0_c': _L0_c, 'L0_wmod': _L0_wmod}
    _x0 = _d['L0_attn_x']
    _d['L0_attn_x'] = jax.random.normal(jax.random.fold_in(jax.random.key(seed), 1), (2, 1024, 128), dtype=_x0.dtype)
    del _x0
    return _d

def reference(L0_attn_x, L0_attn_w_attn, L0_attn_w_proj, L0_ffn_gate_w, L0_ffn_ws_in, L0_ffn_vs_in, L0_ffn_ws_out, L0_ffn_e_win, L0_ffn_e_vin, L0_ffn_e_wout, L0_c, L0_wmod):

    def _L0_attn_ref(x, w_attn, w_proj):
        import jax, jax.numpy as jnp
        import numpy as np
        import math
        D = 128
        H = 16
        HEAD_D = D // H
        T = 256
        B = 4
        Bv, Tv, _ = x.shape
        qkv = x @ w_attn
        q = qkv[..., :D].reshape(Bv, Tv, H, HEAD_D).transpose(0, 2, 1, 3)
        k = qkv[..., D:D + HEAD_D]
        v = qkv[..., D + HEAD_D:]
        scale = 1.0 / math.sqrt(HEAD_D)
        att = jnp.einsum('bhqd,bkd->bhqk', q, k) * scale
        causal = jnp.tril(jnp.ones((Tv, Tv), dtype=bool))
        att = jnp.where(causal[None, None, :, :], att, -jnp.inf)
        att = jax.nn.softmax(att, axis=-1)
        y = jnp.einsum('bhqk,bkd->bhqd', att, v)
        y = y.transpose(0, 2, 1, 3).reshape(Bv, Tv, D)
        return y @ w_proj

    def _L0_ffn_ref(x, gate_w, ws_in, vs_in, ws_out, e_win, e_vin, e_wout):
        import jax, jax.numpy as jnp
        import numpy as np
        B, S, D, H, E, K = (2, 128, 128, 64, 16, 4)
        HS = 2 * H

        def silu(z):
            return z * jax.nn.sigmoid(z)
        b, s, d = x.shape
        T = b * s
        xf = x.reshape(T, d)
        g = jax.nn.sigmoid(xf @ gate_w.T)
        topv, topi = jax.lax.top_k(g, K)
        wn = topv / jnp.sum(topv, axis=-1, keepdims=True)
        combine = jnp.zeros_like(g).at[jnp.arange(T)[:, None], topi].add(wn)
        hin = jnp.einsum('td,edh->eth', xf, e_win)
        vin = jnp.einsum('td,edh->eth', xf, e_vin)
        h = silu(hin) * vin * combine.T[:, :, None]
        routed = jnp.einsum('eth,ehd->td', h, e_wout)
        shared = silu(xf @ ws_in) * (xf @ vs_in) @ ws_out
        return (shared + routed).reshape(b, s, d)
    x = L0_attn_x
    mod = (_silu(L0_c) @ L0_wmod).reshape(L0_c.shape[0], 6, 1, -1)
    sa, ca, ga, sb, cb, gb = (mod[:, 0], mod[:, 1], mod[:, 2], mod[:, 3], mod[:, 4], mod[:, 5])
    ga = (2 * (ga >= 0) - 1) * jnp.maximum(jnp.abs(ga), 0.25)
    gb = (2 * (gb >= 0) - 1) * jnp.maximum(jnp.abs(gb), 0.25)
    h = _layernorm(x, axis=-1) * (1 + ca) + sa
    x = x + ga * _L0_attn_ref(h, L0_attn_w_attn, L0_attn_w_proj)
    h = _layernorm(x, axis=-1) * (1 + cb) + sb
    x = x + gb * _L0_ffn_ref(h, L0_ffn_gate_w, L0_ffn_ws_in, L0_ffn_vs_in, L0_ffn_ws_out, L0_ffn_e_win, L0_ffn_e_vin, L0_ffn_e_wout)
    return x

_drawn_inputs = setup_inputs


def setup_inputs(seed=0):
    import zlib

    import numpy as np

    out = dict(_drawn_inputs(seed))
    spreads = {}
    factors = {}
    for name, (base, spread) in spreads.items():
        noise = np.random.default_rng([zlib.crc32(name.encode()), seed]).standard_normal(out[name].shape)
        drawn = base * np.exp(spread * noise) if base else spread * noise
        out[name] = jnp.asarray(drawn.astype(out[name].dtype))
    for name, factor in factors.items():
        out[name] = (out[name] * factor).astype(out[name].dtype)
    return out
```

```python
import concourse.bass as bass
from concourse import mybir
from contextlib import ExitStack


def adaln_attention_moe_kernel(nc, x_d, w_attn_d, w_proj_d, gate_d, ws_in_d, vs_in_d, ws_out_d,
                               e_win_d, e_vin_d, e_wout_d, c_d, wmod_d, out_d):
    f32, bf16, f32r = mybir.dt.float32, mybir.dt.bfloat16, mybir.dt.float32r
    ALU, ACT, AX = mybir.AluOpType, mybir.ActivationFunctionType, mybir.AxisListType

    B, T, D = x_d.shape
    P = 128
    HD = (w_attn_d.shape[1] - D) // 2
    H = D // HD
    E, _, F = e_win_d.shape
    TOPK = 4
    TB = T // P
    NU = B * TB
    CH = 4 * P
    NC = B * T // CH
    CB = T // CH
    G = 4
    HG = H // G
    SCALE = float(HD) ** -0.5
    EPS = 1e-5
    LOW = -3.0e38
    NBK, NMB, NPB = 3, 3, 3
    FC = E * F // P
    EC = P // F

    def row(i, j):
        return (2 - j) * 32 + i * HD
    KR, SH = 96, 96

    units = [(b, t) for b in range(B) for t in range(TB)]
    jobs = []
    for u, (b, t) in enumerate(units):
        L = (t + 1) * P
        k0 = max(0, L - CH) if L <= CH else CH
        if L > CH:
            jobs += [(u, 0, h, 1, 0, CH, False) for h in range(H)]
        w = L - k0
        n = CH // w
        jobs += [(u, int(k0 > 0), h, min(n, H - h), k0, w, True) for h in range(0, H, n)]
    blocks = [(u, kt, i == 0, i == t) for u, (b, t) in enumerate(units)
              for i, kt in enumerate([t, *range(t)])]
    last_job = [max(j for j in range(len(jobs)) if jobs[j][0] == u) for u in range(NU)]
    merges = [sum(units[w][1] * P + P > CH for w in range(u + 1)) for u in range(NU)]
    first_block = [next(n for n, x in enumerate(blocks) if x[0] == u) for u in range(NU)]
    LEAD = 36
    JOBS_PER_STEP = 1.1

    NW = 4
    plan, pending = [], []
    made = dict(job=0, step=0)
    credit = [0.0]

    def flush(step=None):
        for x in sorted(pending, key=lambda x: x[0]):
            if step is None or x[0] <= step:
                pending.remove(x)
                plan.append(x[1])

    def job(now):
        j = made["job"]
        plan.append(("max", j))
        made["job"] += 1
        u = jobs[j][0]
        if j + 1 == len(jobs) or jobs[j + 1][0] != u:
            plan.append(("merge", u))
            pending.append((now + 2, ("shift", u)))

    plan += [("stats", 0), ("silu",), ("norm", 0), ("cond",), ("stats", 1), ("norm", 1)]
    plan += [(k, 0) for k in ("hT", "q", "k", "v")] + [("gates",)]
    plan += [(k, 1) for k in ("hT", "q", "k", "v")]
    while made["job"] < LEAD:
        job(0)
    flush()
    for c in range(CB, NC):
        pending += [(13 + 21 * (c - CB), ("stats", c)), (19 + 21 * (c - CB), ("norm", c))]
    for c in range(CB, NC):
        for i, k in enumerate(("hT", "q", "k", "v")):
            pending.append(((35 + 32 * (c - CB)) + 3 * i, (k, c)))
    pending += [(48 + 40 * i, ("fetch", i)) for i in range(NW)]
    pending += [(64 + 40 * i + 10 * j, ("split", i, j)) for i in range(NW) for j in range(2)]
    for n, (u, kt, first, last) in enumerate(blocks):
        while made["job"] < len(jobs) and jobs[made["job"]][0] <= u:
            job(made["step"])
        if ("shift", u) in [x[1] for x in pending]:
            flush(10 ** 9)
        for g in range(G):
            plan.append(("scores", n, g))
            made["step"] += 1
            credit[0] += JOBS_PER_STEP
            while credit[0] >= 1:
                credit[0] -= 1
                if made["job"] < len(jobs):
                    job(made["step"])
            flush(made["step"])
        if n:
            plan.append(("pv", n - 1))
            if blocks[n - 1][3]:
                v = blocks[n - 1][0]
                plan.append(("evac", v))
                late = [(3, ("oT", v)), (5, ("yT", v)), (9, ("proj", v))]
                if v % 4 == 3:
                    c = v // 4
                    late += [(12, ("stats2", c)), (14, ("h2", c)), (16, ("route", c)), (20, ("pick", c)),
                             (24, ("count", c)), (30, ("share", c)), (38, ("c3T", c))]
                for d, x in late:
                    pending.append((made["step"] + d, x))
    flush(10 ** 9)
    plan += [("pv", len(blocks) - 1), ("evac", NU - 1)]

    items = [(c, f) for c in range(NC) for f in range(FC + 1)]
    tail = {1: [("oT", NU - 1)], 2: [("yT", NU - 1)], 4: [("proj", NU - 1), ("stats2", NC - 1)],
            6: [("h2", NC - 1)], 8: [("route", NC - 1)], 10: [("pick", NC - 1)], 12: [("count", NC - 1)],
            14: [("share", NC - 1)], 16: [("c3T", NC - 1)]}
    for k, (c, f) in enumerate(items):
        plan.append(("ffn", k))
        plan += tail.get(k, [])
        if c and f in (1, 2):
            plan.append((("gated", "turn")[f - 1], c - 1))
    plan += [("ffn", len(items)), ("ffn", len(items) + 1), ("gated", NC - 1), ("turn", NC - 1)]

    kinds = ("cond", "gates", "hT", "q", "k", "v", "shift", "oT", "yT", "proj", "h2", "route", "c3T", "turn")
    early = {"cond": 1, "gates": 2, "q": 1, "k": 2, "v": 3}
    start = plan.index(("scores", 0, 0))
    at, use, uses = {}, {}, [0] * 4
    for n, x in enumerate(plan):
        if x[0] in kinds:
            at[x] = early.get(x[0], 0) if n < start else 0
            use[x] = uses[at[x]]
            uses[at[x]] += 1

    ctx = ExitStack()
    with ctx:
        def sb(name, shape, dt):
            return ctx.enter_context(nc.sbuf_tensor(name, shape, dt))

        def sem(name):
            return ctx.enter_context(nc.semaphore(name))

        xs = sb("xs", [P, NU, D], f32)
        xn = sb("xn", [P, NU // 2, D], f32)
        hT = sb("hT", [P, NC, CH], f32)
        w_attn = sb("w_attn", [P, D + 2 * HD], f32)
        w_proj = sb("w_proj", [P, D], f32)
        w_projg = sb("w_projg", [P, B, D], f32)
        wmod = sb("wmod", [P, 6, D], f32)
        gate_w = sb("gate_w", [E, D], f32)
        gateT = sb("gateT", [P, E], f32)
        w_piece = sb("w_piece", [P, E * F], f32)
        up_parts = sb("up_parts", [P, 2, FC + 1, 2, P], f32r)
        down_parts = sb("down_parts", [P, 2, FC + 1, D], f32r)
        hT_parts = sb("hT_parts", [P, 2, 2, CH], f32r)
        hc_parts = sb("hc_parts", [P, 2, 3, CH], f32r)
        wq = sb("wq", [P, D], f32)
        wk = sb("wk", [P, KR], f32)
        cT = sb("cT", [P, B], f32)
        csil = sb("csil", [P, 4, B], f32)
        csil_wide = sb("csil_wide", [P, B, P], f32)
        mod = sb("mod", [P, 6, B], f32)
        gs = sb("gs", [P, 2, B], f32)
        gw = sb("gw", [P, 3, B, D], f32)
        stat6 = sb("stat6", [P, NU, 6], f32)
        mv = sb("mv", [P, NU, 2], f32)
        std = sb("std", [P, NU], f32)
        eps = sb("eps", [P, 1], f32)
        rstd = sb("rstd", [P, NU], f32)
        qp = [sb(f"qp{i}", [P, NC, CH], bf16) for i in range(3)]
        rq = sb("rq", [P, CH], f32)
        rk = rq[0:2 * 32, :]
        qa = sb("qa", [P, B, H, T], bf16)
        ka = sb("ka", [P, B, T], bf16)
        va = sb("va", [P, NU, 32], f32)
        mx = sb("mx", [P, NU, 2, H], f32)
        mneg = sb("mneg", [H, 2, 2, P], bf16)
        pr = sb("pr", [P, NPB, G, CH], f32)
        osb = sb("osb", [P, 2, CH], f32)
        rec = sb("rec", [P, 2, H], f32)
        y = sb("y", [P, 2, D], f32)
        yT = sb("yT", [P, 2, P], f32)
        ident = sb("ident", [P, P], f32)
        identb = sb("identb", [P, P], bf16)
        mask = sb("mask", [P, P], bf16)
        sel = sb("sel", [3 * E, FC, P], bf16)
        eg = sb("eg", [P, NU, E], f32)
        flags = qp[0][:, :, :].bitcast(f32).rearrange("p c (k u e) -> p c k u e", k=4, e=E)
        top = sb("top", [P, NU, 8], f32)
        tsum = sb("tsum", [P, 3, NU], f32)
        c3 = qp[1][:, :, 0:4 * 3 * E].rearrange("p c (u s e) -> p c u s e", s=3, e=E)
        c3T = qp[2][0:3 * E, :, :]
        slot = pr[:, :, :, :].rearrange("p n g q -> p (n g) q")
        sl, hv, hc, fT = slot[:, 0:2, :], slot[:, 2:4, :], slot[:, 4:7, :], slot[:, 7:9, :]
        res = slot[:, 9:11, :].rearrange("p n (t d) -> p n t d", d=D)

        bank = [ctx.enter_context(nc.psum_tensor(f"bank{i}", [P, CH], f32)) for i in range(8)]
        score_banks, max_banks, o_bank = bank[0:NBK], bank[NBK:NBK + NMB], bank[6]
        small = [bank[7], o_bank, bank[1], bank[2]]
        hin_banks, vin_banks, share_banks, down_bank = bank[0:2], bank[2:4], bank[4:6], bank[6]

        x_in = [sem(f"x_in{c}") for c in range(NC)]
        w_attn_in, w_proj_in, c_in, cond_in = sem("w_attn_in"), sem("w_proj_in"), sem("c_in"), sem("cond_in")
        q_in = [sem(f"q_in{c}") for c in range(NC)]
        shift_in = [sem(f"shift_in{u}") for u in range(NU)]
        consts, wk_ready, qa_cleared, va_cleared = sem("consts"), sem("wk_ready"), sem("qa_cleared"), sem("va_cleared")
        dve, pool = sem("dve"), sem("pool")
        stats_ready, std_ready, xn_ready = sem("stats_ready"), sem("std_ready"), sem("xn_ready")
        c_exp, csil_ready = sem("c_exp"), sem("csil_ready")
        small_ready = [sem(f"small_ready{i}") for i in range(4)]
        small_read = [sem(f"small_read{i}") for i in range(4)]
        q_hi, k_hi, q_parts, k_done = sem("q_hi"), sem("k_hi"), sem("q_parts"), sem("k_done")
        max_ready, max_read, merged = sem("max_ready"), sem("max_read"), sem("merged")
        scores_ready, exp_done, masked = sem("scores_ready"), sem("exp_done"), sem("masked")
        pv_done, evac_done = sem("pv_done"), sem("evac_done")
        x1_stats, c3_ready = sem("x1_stats"), sem("c3_ready")
        piece_in = [sem(f"piece_in{i}") for i in range(NW)]
        piece_split, h2_split = sem("piece_split"), sem("h2_split")
        hin_ready, vin_ready, comb_ready = sem("hin_ready"), sem("vin_ready"), sem("comb_ready")
        silu_done, prod_done, hid_done = sem("silu_done"), sem("prod_done"), sem("hid_done")
        hid_hi, hid_lo, down_done = sem("hid_hi"), sem("hid_lo"), sem("down_done")
        f_evac = sem("f_evac")
        out_sent = [sem(f"out_sent{c}") for c in range(NC)]

        block = ctx.enter_context(nc.Block())

        @block.sync
        def _(sp):
            xv = x_d.rearrange("b (t p) d -> p (b t) d", p=P)
            sp.dma_start(xs[:, 0:4, :], xv[:, 0:4, :]).then_inc(x_in[0], 16)
            sp.dma_start(w_attn[:, :], w_attn_d).then_inc(w_attn_in, 16)
            for c in range(1, NC):
                sp.dma_start(xs[:, 4 * c:4 * c + 4, :], xv[:, 4 * c:4 * c + 4, :]).then_inc(x_in[c], 16)
            sp.dma_start(gate_w[:, :], gate_d).then_inc(cond_in, 16)
            sp.dma_start(w_proj[:, :], w_proj_d).then_inc(w_proj_in, 16)
            for x in plan:
                if x[0] == "q":
                    c = x[1]
                    b, t0 = c // CB, c % CB * CH
                    sp.wait_ge(q_parts, c + 1)
                    sp.wait_ge(qa_cleared, c + 1)
                    for i in range(3):
                        for j in range(3):
                            r = row(i, j)
                            sp.dma_start(qa[r:r + HD, b, :, t0:t0 + CH],
                                         qp[i][:, c, :]).then_inc(q_in[c], 16)
                if x[0] == "fetch":
                    i = x[1]
                    if i:
                        sp.wait_ge(piece_split, 2 * i)
                    if i < 2:
                        sp.dma_start(w_piece[:, :].rearrange("p (e f) -> p e f", e=E),
                                     (e_win_d, e_vin_d)[i].rearrange("e d f -> d e f")).then_inc(piece_in[i], 16)
                    elif i == 2:
                        sp.dma_start(w_piece[:, :].rearrange("p (c d) -> p c d", d=D),
                                     e_wout_d.rearrange("(c s) f d -> (s f) c d", s=EC)).then_inc(piece_in[i], 16)
                    else:
                        for k, w_d in enumerate((ws_in_d, vs_in_d, ws_out_d)):
                            sp.dma_start(w_piece[:, k * P:(k + 1) * P], w_d).then_inc(piece_in[i], 16)
                if x[0] == "shift":
                    u = x[1]
                    b, t = units[u]
                    sp.wait_ge(small_read[at[x]], use[x] + 1)
                    for s in range(2):
                        sp.dma_start(qa[SH + s:SH + s + 1, b, :, t * P:(t + 1) * P],
                                     mneg[:, u % 2, s, :]).then_inc(shift_in[u], 16)
            ov = out_d.rearrange("b (t p) d -> p (b t) d", p=P)
            for c in range(NC):
                sp.wait_ge(small_read[at["turn", c]], use["turn", c] + 1)
                sp.dma_start(ov[:, 4 * c:4 * c + 4, :], res[:, c % 2, :, :]).then_inc(out_sent[c], 16)
            for c in range(NC):
                sp.wait_ge(out_sent[c], 16)

        @block.gpsimd
        def _(gp):
            steps = [0]

            def own(ins):
                steps[0] += 1
                ins.then_inc(pool, 1)
                return steps[0]

            def identity(m):
                own(gp.memset(m[:, :], 0.0))
                gp.wait_ge(pool, steps[0])
                gp.affine_select(out=m[:, :], in_=m[:, :], compare_op=ALU.not_equal, fill=1.0, base=0,
                                 pattern=[[-1, P]], channel_multiplier=1).then_inc(consts, 1)

            def clear(c):
                b, t0 = c // CB, c % CB * CH
                gp.memset(qa[:, b, :, t0:t0 + CH].bitcast(f32), 0.0).then_inc(qa_cleared, 1)

            identity(ident)
            clear(0)
            identity(identb)
            own(gp.memset(mask[:, :], 0.0))
            gp.wait_ge(pool, steps[0])
            gp.affine_select(out=mask[:, :], in_=mask[:, :], compare_op=ALU.is_ge, fill=LOW, base=0,
                             pattern=[[-1, P]], channel_multiplier=1).then_inc(consts, 1)
            for c in range(1, NC):
                clear(c)
            own(gp.memset(sel[:, :, :], 0.0))
            for i in range(3):
                gp.wait_ge(pool, steps[0])
                ins = gp.affine_select(out=sel[:, :, :], in_=sel[:, :, :], compare_op=ALU.not_equal, fill=1.0,
                                       base=-i * E, pattern=[[-EC, FC], [-1, EC], [0, F]], channel_multiplier=1)
                if i < 2:
                    own(ins)
                else:
                    ins.then_inc(consts, 1)
            def split(parts, whole, done):
                own(gp.tensor_copy(parts[0], whole))
                gp.wait_ge(pool, steps[0])
                gp.tensor_tensor(parts[1], whole, parts[0], ALU.subtract).then_inc(done, 1)

            for x in plan:
                kind = x[0]
                if kind == "split":
                    i, half = x[1:]
                    if half == 0:
                        gp.wait_ge(piece_in[i], 48 if i == 3 else 16)
                    lo = half * 4
                    whole = w_piece[:, :].rearrange("p (f m) -> p f m", m=P)
                    if i < 2:
                        split([up_parts[:, k, 1 + lo:5 + lo, i, :] for k in range(2)], whole[:, lo:lo + 4, :], piece_split)
                    elif i == 2:
                        split([down_parts[:, k, 1 + lo:5 + lo, :] for k in range(2)], whole[:, lo:lo + 4, :], piece_split)
                    elif half == 0:
                        split([up_parts[:, k, 0, :, :] for k in range(2)], whole[:, 0:2, :], piece_split)
                    else:
                        split([down_parts[:, k, 0, :] for k in range(2)], whole[:, 2, :], piece_split)
                elif kind == "h2" and x[1] < 2:
                    c = x[1]
                    gp.wait_ge(small_read[at[x]], use[x] + 1)
                    split([hT_parts[:, i, c, :] for i in range(2)], hT[:, c, :], h2_split)
                elif kind == "ffn" and x[1] < len(items) and items[x[1]][1] == 2 and 0 < items[x[1]][0] < NC - 1:
                    c = items[x[1]][0] + 1
                    gp.wait_ge(small_read[at["h2", c]], use["h2", c] + 1)
                    gp.wait_ge(vin_ready, (c - 1) * (FC + 1))
                    split([hT_parts[:, i, c % 2, :] for i in range(2)], hT[:, c, :], h2_split)
                elif kind == "scores":
                    n, g = x[1:]
                    if blocks[n][2]:
                        gp.wait_ge(exp_done, G * n + g + 1)
                        p4 = pr[:, n % NPB, g, :].rearrange("p (h q) -> p h q", q=P)
                        gp.affine_select(out=p4, in_=p4, compare_op=ALU.is_ge, fill=0.0, base=0,
                                         pattern=[[0, HG], [1, P]], channel_multiplier=-1).then_inc(masked, 1)

        @block.scalar
        def _(act):
            act.dma_start(cT[:, :], c_d.rearrange("b d -> d b"), allow_slow_non_contiguous=True).then_inc(c_in, 16)
            act.dma_start(wmod[:, :, :], wmod_d.rearrange("k (j d) -> k j d", j=6)).then_inc(cond_in, 16)
            step = 0
            for x in plan:
                kind = x[0]
                if kind == "norm":
                    lo, hi = 4 * x[1], 4 * x[1] + 4
                    act.wait_ge(va_cleared, 1)
                    act.wait_ge(stats_ready, x[1] + 1)
                    act.activation(std[:, lo:hi], mv[:, lo:hi, 1], ACT.Sqrt, bias=eps[:, :], scale=1.0).then_inc(std_ready, 1)
                elif kind == "silu":
                    act.wait_ge(c_in, 16)
                    act.activation(csil[:, 0, :], cT[:, :], ACT.Exp, scale=-1.0).then_inc(c_exp, 1)
                elif kind == "hT":
                    c = x[1]
                    b = c // CB
                    act.wait_ge(small_read[at["cond",]], use["cond",] + 1)
                    act.wait_ge(small_ready[at[x]], use[x] + 1)
                    act.activation(hT[:, c, :], small[at[x]][:, :], ACT.Identity, scale=mod[:, 1, b:b + 1],
                                   bias=mod[:, 0, b:b + 1]).then_inc(small_read[at[x]], 1)
                elif kind == "q":
                    c = x[1]
                    act.wait_ge(small_ready[at[x]], use[x] + 1)
                    act.activation(qp[0][:, c, :], small[at[x]][:, :], ACT.Copy).then_inc(q_hi, 1)
                elif kind == "k":
                    c = x[1]
                    b, t0 = c // CB, c % CB * CH
                    act.wait_ge(small_ready[at[x]], use[x] + 1)
                    act.activation(ka[0:KR, b, t0:t0 + CH], small[at[x]][0:KR, :], ACT.Copy).then_inc(k_hi, 1)
                elif kind == "scores":
                    n, g = x[1:]
                    if g == 0 and n >= NPB:
                        act.wait_ge(pv_done, n - NPB + 1)
                    act.wait_ge(scores_ready, step + 1)
                    act.activation(pr[:, n % NPB, g, :], score_banks[step % NBK][:, :], ACT.Exp,
                                   scale=SCALE).then_inc(exp_done, 1)
                    step += 1
                elif kind == "evac":
                    u = x[1]
                    last = first_block[u + 1] if u + 1 < NU else len(blocks)
                    act.wait_ge(pv_done, last)
                    if u >= 2:
                        act.wait_ge(small_ready[at["oT", u - 2]], use["oT", u - 2] + 1)
                    act.activation(osb[:, u % 2, :], o_bank[:, :], ACT.Copy).then_inc(evac_done, 1)
                elif kind == "yT":
                    u = x[1]
                    act.wait_ge(small_ready[at[x]], use[x] + 1)
                    act.activation(yT[:, u % 2, :], small[at[x]][:, 0:P], ACT.Copy).then_inc(small_read[at[x]], 1)

                elif kind == "stats2":
                    lo, hi = 4 * x[1], 4 * x[1] + 4
                    act.wait_ge(x1_stats, hi)
                    act.activation(std[:, lo:hi], mv[:, lo:hi, 1], ACT.Sqrt, bias=eps[:, :], scale=1.0).then_inc(std_ready, 1)
                elif kind == "h2":
                    c = x[1]
                    act.wait_ge(small_ready[at[x]], use[x] + 1)
                    act.activation(hT[:, c, :], small[at[x]][:, :], ACT.Identity, scale=mod[:, 4, c // CB:c // CB + 1],
                                   bias=mod[:, 3, c // CB:c // CB + 1]).then_inc(small_read[at[x]], 1)
                elif kind == "route":
                    c = x[1]
                    act.wait_ge(small_ready[at[x]], use[x] + 1)
                    act.activation(eg[:, 4 * c:4 * c + 4, :], small[at[x]][:, 0:4 * E].rearrange("p (u e) -> p u e", e=E),
                                   ACT.Exp, scale=-1.0).then_inc(small_read[at[x]], 1)
                elif kind == "ffn":
                    k = x[1]
                    if k < len(items):
                        act.wait_ge(hin_ready, k + 1)
                        if k == 0:
                            act.wait_ge(pv_done, len(blocks))
                        if k >= 2:
                            act.wait_ge(prod_done, k - 1)
                        act.activation(sl[:, k % 2, :], hin_banks[k % 2][:, :], ACT.Silu).then_inc(silu_done, 1)
                    if 0 < k <= len(items):
                        k -= 1
                        c, f = items[k]
                        if f == 0:
                            act.wait_ge(prod_done, k + 1)
                        else:
                            act.wait_ge(hid_done, k - c)
                        if k >= 3:
                            act.wait_ge(down_done, k - 2)
                        act.activation(hc_parts[:, 0, k % 3, :], hc[:, k % 3, :], ACT.Copy).then_inc(hid_hi, 1)
                elif kind == "gated":
                    c = x[1]
                    act.wait_ge(down_done, (c + 1) * (FC + 1))
                    if c >= 2:
                        act.wait_ge(small_ready[at["turn", c - 2]], use["turn", c - 2] + 1)
                    act.activation(fT[:, c % 2, :], down_bank[:, :], ACT.Copy, scale=gs[:, 0, c // CB:c // CB + 1]
                                   ).then_inc(f_evac, 1)

        @block.vector
        def _(v):
            steps = [0]

            def own(ins):
                steps[0] += 1
                ins.then_inc(dve, 1)
                v.wait_ge(dve, steps[0])

            v.memset(eps[:, :], EPS).then_inc(va_cleared, 1)
            own(v.memset(va[:, :, :], 0.0))
            v.memset(va[:, :, HD:HD + 1], 1.0).then_inc(va_cleared, 1)
            v.memset(ka[SH:P, :, :], 1.0).then_inc(va_cleared, 1)
            own(v.memset(wk[:, :], 0.0))
            nq = nk = nstd = nxn = ncomb = 0
            for x in plan:
                kind = x[0]
                if kind == "stats":
                    lo, hi = 4 * x[1], 4 * x[1] + 4
                    for u in range(lo, hi):
                        if u % 4 == 0:
                            v.wait_ge(x_in[u // 4], 16)
                        v.bn_stats(stat6[:, u, :], xs[:, u, :]).then_inc(dve, 1)
                        steps[0] += 1
                    v.wait_ge(dve, steps[0])
                    for u in range(lo, hi):
                        ins = v.bn_aggr(mv[:, u, :], stat6[:, u, :])
                    ins.then_inc(stats_ready, 1)
                elif kind == "norm":
                    lo, hi = 4 * x[1], 4 * x[1] + 4
                    nstd += 1
                    v.wait_ge(std_ready, nstd)
                    own(v.reciprocal(rstd[:, lo:hi], std[:, lo:hi]))
                    before = ("h2" if kind == "stats2" and x[1] >= 2 else "hT", (x[1] - 2) % NC)
                    if nstd > 2:
                        v.wait_ge(small_ready[at[before]], use[before] + 1)
                    for u in range(lo, hi):
                        ins = v.tensor_scalar(xn[:, u % (NU // 2), :], xs[:, u, :], mv[:, u, 0:1], rstd[:, u:u + 1],
                                              ALU.subtract, ALU.mult)
                        if u % 4 == 3:
                            ins.then_inc(xn_ready, 1)
                elif kind == "silu":
                    v.wait_ge(c_exp, 1)
                    own(v.tensor_scalar(csil[:, 1, :], csil[:, 0, :], 1.0, None, ALU.add))
                    own(v.reciprocal(csil[:, 2, :], csil[:, 1, :]))
                    own(v.tensor_tensor(csil[:, 3, :], cT[:, :], csil[:, 2, :], ALU.mult))
                    v.tensor_copy(csil_wide[:, :, :], csil[:, 3, :].unsqueeze(2).broadcast_to([P, B, P])
                                  ).then_inc(csil_ready, 1)
                elif kind == "cond":
                    v.wait_ge(w_attn_in, 16)
                    v.tensor_copy(wq[:, :].rearrange("p (d h) -> p d h", h=H),
                                  w_attn[:, 0:D].rearrange("p (h d) -> p d h", d=HD)).then_inc(wk_ready, 1)
                    v.tensor_copy(wk[:, :].rearrange("p (j i d) -> p j i d", i=4, d=HD)[:, :, 0:3, :],
                                  w_attn[:, D:D + HD].unsqueeze(1).unsqueeze(1).broadcast_to([P, 3, 3, HD])
                                  ).then_inc(wk_ready, 1)
                    v.wait_ge(small_ready[at[x]], use[x] + 1)
                    own(v.tensor_copy(mod[:, :, :], small[at[x]][:, 0:6 * B].rearrange("p (j b) -> p j b", b=B)))
                    for j in (1, 4):
                        own(v.tensor_scalar(mod[:, j, :], mod[:, j, :], 1.0, None, ALU.add))
                    own(v.tensor_scalar(gs[:, 0, :], mod[:, 5, :], 0.0, 2.0, ALU.is_ge, ALU.mult))
                    own(v.tensor_scalar(gs[:, 1, :], mod[:, 5, :], -1.0, None, ALU.mult))
                    own(v.tensor_tensor(gs[:, 1, :], gs[:, 1, :], mod[:, 5, :], ALU.max))
                    own(v.tensor_scalar(gs[:, 1, :], gs[:, 1, :], 0.25, None, ALU.max))
                    v.scalar_tensor_tensor(gs[:, 0, :], gs[:, 0, :], -1.0, gs[:, 1, :], ALU.add, ALU.mult
                                           ).then_inc(small_read[at[x]], 1)
                elif kind == "gates":
                    v.wait_ge(small_ready[at[x]], use[x] + 1)
                    ga = small[at[x]][:, 0:B * D].rearrange("p (b d) -> p b d", b=B)
                    own(v.tensor_copy(gw[:, 0, :, :], ga))
                    own(v.tensor_scalar(gw[:, 1, :, :], gw[:, 0, :, :], 0.0, 2.0, ALU.is_ge, ALU.mult))
                    own(v.tensor_scalar(gw[:, 2, :, :], gw[:, 0, :, :], -1.0, None, ALU.mult))
                    own(v.tensor_tensor(gw[:, 2, :, :], gw[:, 2, :, :], gw[:, 0, :, :], ALU.max))
                    own(v.tensor_scalar(gw[:, 2, :, :], gw[:, 2, :, :], 0.25, None, ALU.max))
                    own(v.scalar_tensor_tensor(gw[:, 0, :, :], gw[:, 1, :, :], -1.0, gw[:, 2, :, :], ALU.add, ALU.mult))
                    own(v.tensor_copy(gateT[:, :], small[at[x]][:, B * D:B * D + E]))
                    v.wait_ge(w_proj_in, 16)
                    v.tensor_tensor(w_projg[:, :, :], gw[:, 0, :, :], w_proj[:, :].unsqueeze(1).broadcast_to([P, B, D]),
                                    ALU.mult).then_inc(small_read[at[x]], 1)
                elif kind == "q":
                    c = x[1]
                    nq += 1
                    v.wait_ge(q_hi, nq)
                    ins = v.tensor_tensor(rq[:, :], small[at[x]][:, :], qp[0][:, c, :], ALU.subtract)
                    ins.then_inc(small_read[at[x]], 1)
                    v.wait_ge(small_read[at[x]], use[x] + 1)
                    own(v.tensor_copy(qp[1][:, c, :], rq[:, :]))
                    v.tensor_tensor(qp[2][:, c, :], rq[:, :], qp[1][:, c, :], ALU.subtract).then_inc(q_parts, 1)
                    v.wait_ge(q_parts, nq)
                elif kind == "k":
                    c = x[1]
                    nk += 1
                    b, t0 = c // CB, c % CB * CH
                    kc = ka[:, b, t0:t0 + CH]
                    v.wait_ge(k_hi, nk)
                    v.tensor_tensor(rk[:, :], small[at[x]][0:64, :], kc[0:64], ALU.subtract).then_inc(small_read[at[x]], 1)
                    v.wait_ge(small_read[at[x]], use[x] + 1)
                    own(v.tensor_copy(kc[0:64], rk[:, :]))
                    v.tensor_tensor(kc[0:32], rk[0:32, :], kc[0:32], ALU.subtract).then_inc(k_done, 1)
                    v.wait_ge(k_done, nk)
                elif kind == "v":
                    c = x[1]
                    v.wait_ge(small_ready[at[x]], use[x] + 1)
                    v.tensor_copy(va[:, 4 * c:4 * c + 4, 0:HD], small[at[x]][:, 0:4 * HD].rearrange("p (t d) -> p t d", d=HD)
                                  ).then_inc(small_read[at[x]], 1)
                elif kind == "max":
                    j = x[1]
                    u, part, h0, nh, k0, w, m = jobs[j]
                    v.wait_ge(max_ready, j + 1)
                    v.tensor_reduce(mx[:, u, part, h0:h0 + nh],
                                    max_banks[j % NMB][:, 0:nh * w].rearrange("p (h k) -> p h k", k=w),
                                    AX.X, ALU.max).then_inc(max_read, 1)
                elif kind == "merge":
                    u = x[1]
                    if units[u][1] * P + P > CH:
                        v.wait_ge(max_read, last_job[u] + 1)
                        v.tensor_tensor(mx[:, u, 0, :], mx[:, u, 0, :], mx[:, u, 1, :], ALU.max).then_inc(merged, 1)
                elif kind == "shift":
                    u = x[1]
                    v.wait_ge(small_ready[at[x]], use[x] + 1)
                    if u >= 2:
                        v.wait_ge(shift_in[u - 2], 32)
                    own(v.tensor_scalar(mneg[:, u % 2, 0, :], small[at[x]][0:H, 0:P], -1.0, None, ALU.mult))
                    v.scalar_tensor_tensor(mneg[:, u % 2, 1, :], small[at[x]][0:H, 0:P], -1.0, mneg[:, u % 2, 0, :],
                                           ALU.mult, ALU.subtract).then_inc(small_read[at[x]], 1)
                elif kind == "oT":
                    u = x[1]
                    v.wait_ge(small_ready[at[x]], use[x] + 1)
                    o = small[at[x]][:, :].rearrange("p (h g c) -> p h g c", h=HG, g=G)
                    r = rec[:, u % 2, :].rearrange("p (h g) -> p h g", h=HG)
                    own(v.reciprocal(r, o[:, :, :, HD]))
                    v.tensor_tensor(y[:, u % 2, :].rearrange("p (g h d) -> p h g d", h=HG, g=G), o[:, :, :, 0:HD],
                                    r.unsqueeze(3).broadcast_to([P, HG, G, HD]), ALU.mult).then_inc(small_read[at[x]], 1)
                elif kind == "proj":
                    u = x[1]
                    v.wait_ge(small_ready[at[x]], use[x] + 1)
                    v.tensor_tensor(xs[:, u, :], xs[:, u, :], small[at[x]][:, 0:D], ALU.add).then_inc(small_read[at[x]], 1)
                    v.wait_ge(small_read[at[x]], use[x] + 1)
                    own(v.bn_stats(stat6[:, u, :], xs[:, u, :]))
                    v.bn_aggr(mv[:, u, :], stat6[:, u, :]).then_inc(x1_stats, 1)

                elif kind == "stats2":
                    lo, hi = 4 * x[1], 4 * x[1] + 4
                    nstd += 1
                    v.wait_ge(std_ready, nstd)
                    own(v.reciprocal(rstd[:, lo:hi], std[:, lo:hi]))
                    before = ("h2" if kind == "stats2" and x[1] >= 2 else "hT", (x[1] - 2) % NC)
                    if nstd > 2:
                        v.wait_ge(small_ready[at[before]], use[before] + 1)
                    for u in range(lo, hi):
                        ins = v.tensor_scalar(xn[:, u % (NU // 2), :], xs[:, u, :], mv[:, u, 0:1], rstd[:, u:u + 1],
                                              ALU.subtract, ALU.mult)
                    ins.then_inc(xn_ready, 1)
                elif kind == "route":
                    v.wait_ge(q_in[x[1]], 9 * 16)
                    us = slice(4 * x[1], 4 * x[1] + 4)
                    g = eg[:, us, :]
                    v.wait_ge(small_read[at[x]], use[x] + 1)
                    own(v.tensor_scalar(g, g, 1.0, None, ALU.add))
                    own(v.reciprocal(g, g))
                    for u in range(4 * x[1], 4 * x[1] + 4):
                        steps[0] += 1
                        v.max(top[:, u, :], eg[:, u, :]).then_inc(dve, 1)
                    v.wait_ge(dve, steps[0])
                elif kind == "pick":
                    us = slice(4 * x[1], 4 * x[1] + 4)
                    fourth = top[:, us, TOPK - 1:TOPK].broadcast_to([P, 4, E])
                    steps[0] += 2
                    v.tensor_tensor(flags[:, x[1], 0], eg[:, us, :], fourth, ALU.is_gt).then_inc(dve, 1)
                    v.tensor_tensor(flags[:, x[1], 1], eg[:, us, :], fourth, ALU.is_equal).then_inc(dve, 1)
                    v.wait_ge(dve, steps[0])
                    own(v.tensor_reduce(tsum[:, 0, us], flags[:, x[1], 0], AX.X, ALU.add))
                    steps[0] += 1
                    v.tensor_scalar(tsum[:, 0, us], tsum[:, 0, us], -1.0, float(TOPK), ALU.mult, ALU.add).then_inc(dve, 1)
                    own(v.tensor_reduce(tsum[:, 1, us], top[:, us, 0:TOPK], AX.X, ALU.add))
                    own(v.reciprocal(tsum[:, 2, us], tsum[:, 1, us]))
                elif kind == "count":
                    us = slice(4 * x[1], 4 * x[1] + 4)
                    a, d, s = flags[:, x[1], 1], 1, 0
                    while d < E:
                        to = flags[:, x[1], 2 + s]
                        steps[0] += 2
                        v.tensor_copy(to[:, :, 0:d], a[:, :, 0:d]).then_inc(dve, 1)
                        v.tensor_tensor(to[:, :, d:E], a[:, :, d:E], a[:, :, 0:E - d], ALU.add).then_inc(dve, 1)
                        v.wait_ge(dve, steps[0])
                        a, d, s = to, 2 * d, 1 - s
                    own(v.tensor_tensor(a, a, tsum[:, 0, us].unsqueeze(2).broadcast_to([P, 4, E]), ALU.is_le))
                    own(v.tensor_tensor(flags[:, x[1], 1], flags[:, x[1], 1], a, ALU.mult))
                elif kind == "share":
                    us = slice(4 * x[1], 4 * x[1] + 4)
                    w = flags[:, x[1], 0]
                    own(v.tensor_tensor(w, w, flags[:, x[1], 1], ALU.add))
                    own(v.tensor_tensor(w, w, eg[:, us, :], ALU.mult))
                    own(v.tensor_tensor(w, w, tsum[:, 2, us].unsqueeze(2).broadcast_to([P, 4, E]), ALU.mult))
                    own(v.tensor_copy(c3[:, x[1], :, 0, :], w))
                    own(v.tensor_tensor(w, w, c3[:, x[1], :, 0, :], ALU.subtract))
                    own(v.tensor_copy(c3[:, x[1], :, 1, :], w))
                    v.tensor_tensor(c3[:, x[1], :, 2, :], w, c3[:, x[1], :, 1, :], ALU.subtract).then_inc(c3_ready, 1)
                elif kind == "c3T":
                    c = x[1]
                    v.wait_ge(small_ready[at[x]], use[x] + 1)
                    v.tensor_copy(c3T[:, c, :], small[at[x]][0:3 * E, 0:CH // 2].bitcast(bf16)
                                  ).then_inc(small_read[at[x]], 1)
                elif kind == "ffn":
                    k = x[1]
                    if k < len(items):
                        f = items[k][1]
                        if k >= 3:
                            v.wait_ge(hid_lo, k - 2)
                        v.wait_ge(vin_ready, k + 1)
                        v.wait_ge(silu_done, k + 1)
                        to = hc[:, k % 3, :] if f == 0 else hv[:, k % 2, :]
                        v.tensor_tensor(to, sl[:, k % 2, :], vin_banks[k % 2][:, :], ALU.mult).then_inc(prod_done, 1)
                    if 0 < k <= len(items):
                        v.wait_ge(hid_hi, k)
                        v.tensor_tensor(hc_parts[:, 1, (k - 1) % 3, :], hc[:, (k - 1) % 3, :],
                                        hc_parts[:, 0, (k - 1) % 3, :], ALU.subtract).then_inc(hid_lo, 1)
                    if k < len(items) and f:
                        ncomb += 1
                        v.wait_ge(prod_done, k + 1)
                        v.wait_ge(comb_ready, ncomb)
                        v.tensor_tensor(hc[:, k % 3, :], hv[:, k % 2, :], share_banks[ncomb % 2][:, :], ALU.mult
                                        ).then_inc(hid_done, 1)
                elif kind == "turn":
                    c = x[1]
                    v.wait_ge(small_ready[at[x]], use[x] + 1)
                    if c >= 2:
                        v.wait_ge(out_sent[c - 2], 16)
                    v.tensor_tensor(res[:, c % 2, :, :], small[at[x]][:, :].rearrange("p (t d) -> p t d", d=D),
                                    xs[:, 4 * c:4 * c + 4, :], ALU.add).then_inc(small_read[at[x]], 1)

        @block.tensor
        def _(pe):
            def mm(out, lhsT, rhs, start=True, stop=True):
                return pe.matmul(out, lhsT, rhs, start=start, stop=stop, skip_group_check=True)

            def small_free(x):
                if use[x]:
                    pe.wait_ge(small_read[at[x]], use[x])

            PARTS = ((0, 0), (1, 0), (0, 1))
            step = ncomb = 0
            pe.wait_ge(consts, 1)
            for x in plan:
                kind = x[0]
                if kind == "cond":
                    small_free(x)
                    pe.wait_ge(cond_in, 32)
                    pe.wait_ge(csil_ready, 1)
                    for j in range(6):
                        ins = mm(small[at[x]][:, B * j:B * j + B], wmod[:, j, :], csil[:, 3, :])
                    ins.then_inc(small_ready[at[x]], 1)
                elif kind == "gates":
                    small_free(x)
                    for b in range(B):
                        ins = mm(small[at[x]][:, b * D:(b + 1) * D], csil_wide[:, b, :], wmod[:, 2, :])
                    pe.wait_ge(cond_in, 32)
                    ins = pe.transpose(small[at[x]][:, B * D:B * D + E], gate_w[:, :], ident[0:E, 0:E])
                    ins.then_inc(small_ready[at[x]], 1)
                elif kind == "hT":
                    c = x[1]
                    pe.wait_ge(xn_ready, c + 1)
                    small_free(x)
                    for i in range(4):
                        ins = pe.transpose(small[at[x]][:, i * P:(i + 1) * P], xn[:, 4 * (c % 2) + i, :], ident[:, :])
                    ins.then_inc(small_ready[at[x]], 1)
                elif kind == "q":
                    c = x[1]
                    pe.wait_ge(small_read[at["hT", c]], use["hT", c] + 1)
                    small_free(x)
                    pe.wait_ge(wk_ready, 1)
                    mm(small[at[x]][:, :], wq[:, :], hT[:, c, :]).then_inc(small_ready[at[x]], 1)
                elif kind == "k":
                    c = x[1]
                    pe.wait_ge(wk_ready, 2)
                    small_free(x)
                    mm(small[at[x]][0:KR, :], wk[:, :], hT[:, c, :]).then_inc(small_ready[at[x]], 1)
                elif kind == "v":
                    c = x[1]
                    small_free(x)
                    for i in range(4):
                        ins = mm(small[at[x]][:, i * HD:(i + 1) * HD], hT[:, c, i * P:(i + 1) * P], w_attn[:, D + HD:D + 2 * HD])
                    ins.then_inc(small_ready[at[x]], 1)
                elif kind == "max":
                    j = x[1]
                    u, part, h0, nh, k0, w, m = jobs[j]
                    b, t = units[u]
                    pe.wait_ge(q_in[u // 4], 9 * 16)
                    pe.wait_ge(k_done, u // 4 + 1)
                    pe.wait_ge(va_cleared, 3)
                    if j >= NMB:
                        pe.wait_ge(max_read, j - NMB + 1)
                    for i in range(nh):
                        ins = mm(max_banks[j % NMB][:, i * w:(i + 1) * w], qa[:, b, h0 + i, t * P:(t + 1) * P],
                                 ka[:, b, k0:k0 + w], stop=not m)
                        if m:
                            if j == 0:
                                pe.wait_ge(consts, 3)
                            ins = mm(max_banks[j % NMB][:, (i + 1) * w - P:(i + 1) * w], identb[:, :], mask[:, :],
                                     start=False)
                    ins.then_inc(max_ready, 1)
                elif kind == "shift":
                    u = x[1]
                    pe.wait_ge(max_read, last_job[u] + 1)
                    if units[u][1] * P + P > CH:
                        pe.wait_ge(merged, merges[u])
                    small_free(x)
                    pe.transpose(small[at[x]][0:H, 0:P], mx[:, u, 0, :], ident[:, :]).then_inc(small_ready[at[x]], 1)
                elif kind == "scores":
                    n, g = x[1:]
                    u, kt, first, last = blocks[n]
                    b, t = units[u]
                    if first and g == 0:
                        pe.wait_ge(shift_in[u], 32)
                    if step == 0:
                        for i in range(1, 4):
                            pe.wait_ge(small_read[i], uses[i])
                    if step >= NBK:
                        pe.wait_ge(exp_done, step - NBK + 1)
                    mm(score_banks[step % NBK][:, :].rearrange("p (h q) -> p h q", q=P),
                       ka[:, b, kt * P:(kt + 1) * P], qa[:, b, g * HG:(g + 1) * HG, t * P:(t + 1) * P]
                       ).then_inc(scores_ready, 1)
                    step += 1
                elif kind == "pv":
                    n = x[1]
                    u, kt, first, last = blocks[n]
                    b, t = units[u]
                    if first:
                        pe.wait_ge(masked, G * (u + 1))
                        if n:
                            pe.wait_ge(evac_done, u)
                        pe.wait_ge(small_read[at["v", u // 4]], use["v", u // 4] + 1)
                    else:
                        pe.wait_ge(exp_done, G * (n + 1))
                    for g in range(G):
                        ins = mm(o_bank[32 * g:32 * g + 32, :], va[:, b * TB + kt, :], pr[:, n % NPB, g, :],
                                 start=first, stop=last)
                    ins.then_inc(pv_done, 1)
                elif kind == "oT":
                    u = x[1]
                    pe.wait_ge(evac_done, u + 1)
                    small_free(x)
                    for i in range(HG):
                        ins = pe.transpose(small[at[x]][:, i * P:(i + 1) * P], osb[:, u % 2, i * P:(i + 1) * P], ident[:, :])
                    ins.then_inc(small_ready[at[x]], 1)
                elif kind == "yT":
                    u = x[1]
                    pe.wait_ge(small_read[at["oT", u]], use["oT", u] + 1)
                    small_free(x)
                    pe.transpose(small[at[x]][:, 0:P], y[:, u % 2, :], ident[:, :]).then_inc(small_ready[at[x]], 1)
                elif kind == "proj":
                    u = x[1]
                    pe.wait_ge(small_read[at["gates",]], use["gates",] + 1)
                    pe.wait_ge(small_read[at["yT", u]], use["yT", u] + 1)
                    small_free(x)
                    mm(small[at[x]][:, 0:D], yT[:, u % 2, :], w_projg[:, units[u][0], :]).then_inc(small_ready[at[x]], 1)

                elif kind == "h2":
                    c = x[1]
                    pe.wait_ge(xn_ready, NC + c + 1)
                    small_free(x)
                    for i in range(4):
                        ins = pe.transpose(small[at[x]][:, i * P:(i + 1) * P], xn[:, 4 * (c % 2) + i, :], ident[:, :])
                    ins.then_inc(small_ready[at[x]], 1)
                elif kind == "route":
                    c = x[1]
                    pe.wait_ge(small_read[at["h2", c]], use["h2", c] + 1)
                    small_free(x)
                    for i in range(4):
                        ins = mm(small[at[x]][:, i * E:(i + 1) * E], hT[:, c, i * P:(i + 1) * P], gateT[:, :])
                    ins.then_inc(small_ready[at[x]], 1)
                elif kind == "c3T":
                    c = x[1]
                    pe.wait_ge(c3_ready, c + 1)
                    small_free(x)
                    for i in range(4):
                        ins = pe.transpose(small[at[x]][0:3 * E, i * P // 2:(i + 1) * P // 2].bitcast(bf16),
                                           c3[:, c, i, :, :].rearrange("p s e -> p (s e)"), identb[:, :])
                    ins.then_inc(small_ready[at[x]], 1)
                elif kind == "ffn":
                    k = x[1]
                    if k == 0:
                        pe.wait_ge(piece_split, 2 * NW)
                        pe.wait_ge(exp_done, G * len(blocks))
                        pe.wait_ge(max_read, len(jobs))
                        pe.wait_ge(consts, 4)
                    if k < len(items):
                        c, f = items[k]
                        pe.wait_ge(h2_split, c + 1)
                        if k >= 2:
                            pe.wait_ge(silu_done, k - 1)
                        for out, wh, done in ((hin_banks, 0, hin_ready), (vin_banks, 1, vin_ready)):
                            if k >= 2 and wh:
                                pe.wait_ge(prod_done, k - 1)
                            for n, (i, j) in enumerate(PARTS):
                                ins = mm(out[k % 2][:, :], up_parts[:, i, f, wh, :], hT_parts[:, j, c % 2, :],
                                         start=n == 0, stop=n == len(PARTS) - 1)
                            ins.then_inc(done, 1)
                        if f:
                            ncomb += 1
                            pe.wait_ge(small_read[at["c3T", c]], use["c3T", c] + 1)
                            if ncomb > 2:
                                pe.wait_ge(hid_done, ncomb - 2)
                            mm(share_banks[ncomb % 2][:, :], sel[:, f - 1, :], c3T[:, c, :]
                               ).then_inc(comb_ready, 1)
                    if k >= 2:
                        k -= 2
                        c, f = items[k]
                        pe.wait_ge(hid_lo, k + 1)
                        if f == 0:
                            pe.wait_ge(evac_done, NU)
                            if c:
                                pe.wait_ge(f_evac, c)
                        for n, (i, j) in enumerate(PARTS):
                            ins = mm(down_bank[:, :], down_parts[:, i, f, :], hc_parts[:, j, k % 3, :],
                                     start=f == 0 and n == 0, stop=f == FC and n == len(PARTS) - 1)
                        ins.then_inc(down_done, 1)
                elif kind == "turn":
                    c = x[1]
                    pe.wait_ge(f_evac, c + 1)
                    small_free(x)
                    for i in range(4):
                        ins = pe.transpose(small[at[x]][:, i * P:(i + 1) * P], fT[:, c % 2, i * P:(i + 1) * P], ident[:, :])
                    ins.then_inc(small_ready[at[x]], 1)


_INS = ["L0_attn_x", "L0_attn_w_attn", "L0_attn_w_proj", "L0_ffn_gate_w", "L0_ffn_ws_in", "L0_ffn_vs_in",
        "L0_ffn_ws_out", "L0_ffn_e_win", "L0_ffn_e_vin", "L0_ffn_e_wout", "L0_c", "L0_wmod"]


def kernel(**inputs):
    import numpy as _np
    import concourse.bacc as _bacc
    from concourse import mybir as _mybir
    from concourse.bass_utils import run_bass_kernel_spmd as _run

    nc = _bacc.Bacc("TRN2", target_bir_lowering=False, num_devices=1)
    arrays, args = {}, []
    for name in _INS:
        a = _np.ascontiguousarray(inputs[name])
        arrays[f"in_{name}"] = a
        args.append(nc.dram_tensor(f"in_{name}", a.shape, _mybir.dt.from_np(a.dtype), kind="ExternalInput").ap())
    x = inputs["L0_attn_x"]
    args.append(nc.dram_tensor("out_x", x.shape, _mybir.dt.float32, kind="ExternalOutput").ap())
    adaln_attention_moe_kernel(nc, *args)
    r = _run(nc, [arrays], core_ids=[0])
    return r.results[0]["out_x"]
```
